# Optimizing a Trainium2 kernel written in Bass

```python
import numpy as np
import jax
import jax.numpy as jnp

def _softmax(x, axis=-1):
    return jax.nn.softmax(x, axis=axis)

def _gelu(x):
    return jax.nn.gelu(x, approximate=True)

def _silu(x):
    return jax.nn.silu(x)

def _sigmoid(x):
    return jax.nn.sigmoid(x)

def _layernorm(x, axis=-1, eps=1e-05):
    m = jnp.mean(x, axis=axis, keepdims=True)
    v = jnp.var(x, axis=axis, keepdims=True)
    return (x - m) / jnp.sqrt(v + eps)

def _scatter_add(tgt, idx, src, axis=0):
    return tgt.at[idx].add(src)

def _segment_sum(src, seg, n):
    return jax.ops.segment_sum(src, seg, n)
kernel_name = 'mk_rec_standalone_d1_rec_r8_08f6ec'

def setup_inputs(seed: int=0):
    np.random.seed(seed)
    _w = jnp.asarray

    def _rec_inputs():
        import jax
        import jax.numpy as jnp
        _rk = jax.random.key(seed)
        r_z = jax.random.randint(jax.random.fold_in(_rk, 1), (4096, 48), 0, 48, jnp.int32)
        return r_z
    r_z = _rec_inputs()

    def _L0_rec_setup():
        import jax, jax.numpy as jnp
        import numpy as np
        B, N, C = (4096, 48, 48)
        HD1, HD2, NRD = (512, 256, 2)
        EPS = 1e-05

        def _bn(x, g, b, m, v):
            return g * (x - m) * jax.lax.rsqrt(v + EPS) + b
        key = jax.random.key(seed)
        ks = jax.random.split(key, 8)
        s = 0.02
        inp = {'z': jax.random.randint(ks[0], (B, N), 0, C), 'w1': jax.random.normal(ks[1], (HD1, N * C), jnp.float32) * s, 'b1': jnp.zeros((HD1,), jnp.float32), 'g1': jnp.ones((HD1,), jnp.float32), 'be1': jnp.zeros((HD1,), jnp.float32), 'm1': jnp.zeros((HD1,), jnp.float32), 'v1': jnp.ones((HD1,), jnp.float32), 'w2': jax.random.normal(ks[2], (HD2, HD1), jnp.float32) * s, 'b2': jnp.zeros((HD2,), jnp.float32), 'g2': jnp.ones((HD2,), jnp.float32), 'be2': jnp.zeros((HD2,), jnp.float32), 'm2': jnp.zeros((HD2,), jnp.float32), 'v2': jnp.ones((HD2,), jnp.float32), 'rw1': jax.random.normal(ks[3], (NRD, HD2, HD2), jnp.float32) * s, 'rb1': jnp.zeros((NRD, HD2), jnp.float32), 'rg1': jnp.ones((NRD, HD2), jnp.float32), 'rbe1': jnp.zeros((NRD, HD2), jnp.float32), 'rm1': jnp.zeros((NRD, HD2), jnp.float32), 'rv1': jnp.ones((NRD, HD2), jnp.float32), 'rw2': jax.random.normal(ks[4], (NRD, HD2, HD2), jnp.float32) * s, 'rb2': jnp.zeros((NRD, HD2), jnp.float32), 'rg2': jnp.ones((NRD, HD2), jnp.float32), 'rbe2': jnp.zeros((NRD, HD2), jnp.float32), 'rm2': jnp.zeros((NRD, HD2), jnp.float32), 'rv2': jnp.ones((NRD, HD2), jnp.float32), 'wout': jax.random.normal(ks[5], (1, HD2), jnp.float32) * s, 'bout': jnp.zeros((1,), jnp.float32)}
        return inp
    _L0_rec_all = _L0_rec_setup()
    _L0_rec_in = {k: v for k, v in _L0_rec_all.items() if k in ('w1', 'b1', 'g1', 'be1', 'm1', 'v1', 'w2', 'b2', 'g2', 'be2', 'm2', 'v2', 'rw1', 'rb1', 'rg1', 'rbe1', 'rm1', 'rv1', 'rw2', 'rb2', 'rg2', 'rbe2', 'rm2', 'rv2', 'wout', 'bout')}
    del _L0_rec_all
    return {'r_z': r_z, 'L0_rec_w1': _L0_rec_in['w1'], 'L0_rec_b1': _L0_rec_in['b1'], 'L0_rec_g1': _L0_rec_in['g1'], 'L0_rec_be1': _L0_rec_in['be1'], 'L0_rec_m1': _L0_rec_in['m1'], 'L0_rec_v1': _L0_rec_in['v1'], 'L0_rec_w2': _L0_rec_in['w2'], 'L0_rec_b2': _L0_rec_in['b2'], 'L0_rec_g2': _L0_rec_in['g2'], 'L0_rec_be2': _L0_rec_in['be2'], 'L0_rec_m2': _L0_rec_in['m2'], 'L0_rec_v2': _L0_rec_in['v2'], 'L0_rec_rw1': _L0_rec_in['rw1'], 'L0_rec_rb1': _L0_rec_in['rb1'], 'L0_rec_rg1': _L0_rec_in['rg1'], 'L0_rec_rbe1': _L0_rec_in['rbe1'], 'L0_rec_rm1': _L0_rec_in['rm1'], 'L0_rec_rv1': _L0_rec_in['rv1'], 'L0_rec_rw2': _L0_rec_in['rw2'], 'L0_rec_rb2': _L0_rec_in['rb2'], 'L0_rec_rg2': _L0_rec_in['rg2'], 'L0_rec_rbe2': _L0_rec_in['rbe2'], 'L0_rec_rm2': _L0_rec_in['rm2'], 'L0_rec_rv2': _L0_rec_in['rv2'], 'L0_rec_wout': _L0_rec_in['wout'], 'L0_rec_bout': _L0_rec_in['bout']}

def reference(r_z, L0_rec_w1, L0_rec_b1, L0_rec_g1, L0_rec_be1, L0_rec_m1, L0_rec_v1, L0_rec_w2, L0_rec_b2, L0_rec_g2, L0_rec_be2, L0_rec_m2, L0_rec_v2, L0_rec_rw1, L0_rec_rb1, L0_rec_rg1, L0_rec_rbe1, L0_rec_rm1, L0_rec_rv1, L0_rec_rw2, L0_rec_rb2, L0_rec_rg2, L0_rec_rbe2, L0_rec_rm2, L0_rec_rv2, L0_rec_wout, L0_rec_bout):
    import jax
    import jax.numpy as jnp

    def _L0_rec_ref(z, w1, b1, g1, be1, m1, v1, w2, b2, g2, be2, m2, v2, rw1, rb1, rg1, rbe1, rm1, rv1, rw2, rb2, rg2, rbe2, rm2, rv2, wout, bout):
        import jax, jax.numpy as jnp
        import numpy as np
        B, N, C = (4096, 48, 48)
        HD1, HD2, NRD = (512, 256, 2)
        EPS = 1e-05

        def _bn(x, g, b, m, v):
            return g * (x - m) * jax.lax.rsqrt(v + EPS) + b
        oh = jax.nn.one_hot(z, C, dtype=jnp.float32).reshape(B, N * C)
        x = oh @ w1.T + b1
        x = jax.nn.relu(_bn(x, g1, be1, m1, v1))
        x = x @ w2.T + b2
        x = jax.nn.relu(_bn(x, g2, be2, m2, v2))
        for i in range(NRD):
            r = x
            h = jax.nn.relu(_bn(x @ rw1[i].T + rb1[i], rg1[i], rbe1[i], rm1[i], rv1[i]))
            h = _bn(h @ rw2[i].T + rb2[i], rg2[i], rbe2[i], rm2[i], rv2[i])
            x = jax.nn.relu(h + r)
        return (x @ wout.T + bout).reshape(-1)
    y = _L0_rec_ref(r_z, L0_rec_w1, L0_rec_b1, L0_rec_g1, L0_rec_be1, L0_rec_m1, L0_rec_v1, L0_rec_w2, L0_rec_b2, L0_rec_g2, L0_rec_be2, L0_rec_m2, L0_rec_v2, L0_rec_rw1, L0_rec_rb1, L0_rec_rg1, L0_rec_rbe1, L0_rec_rm1, L0_rec_rv1, L0_rec_rw2, L0_rec_rb2, L0_rec_rg2, L0_rec_rbe2, L0_rec_rm2, L0_rec_rv2, L0_rec_wout, L0_rec_bout)
    return y

_drawn_inputs = setup_inputs


def setup_inputs(seed=0):
    import zlib

    import numpy as np

    out = dict(_drawn_inputs(seed))
    spreads = {'L0_rec_b1': (0.0, 0.1),
     'L0_rec_g1': (1.0, 0.6),
     'L0_rec_be1': (0.0, 0.1),
     'L0_rec_m1': (0.0, 0.1),
     'L0_rec_v1': (1.0, 0.6),
     'L0_rec_b2': (0.0, 0.1),
     'L0_rec_g2': (1.0, 0.2),
     'L0_rec_be2': (0.0, 0.1),
     'L0_rec_m2': (0.0, 0.1),
     'L0_rec_v2': (1.0, 0.536),
     'L0_rec_rb1': (0.0, 0.8),
     'L0_rec_rg1': (1.0, 0.6),
     'L0_rec_rbe1': (0.0, 0.1),
     'L0_rec_rm1': (0.0, 0.738),
     'L0_rec_rv1': (1.0, 0.6),
     'L0_rec_rb2': (0.0, 0.326),
     'L0_rec_rg2': (1.0, 0.2),
     'L0_rec_rbe2': (0.0, 0.1),
     'L0_rec_rm2': (0.0, 0.1),
     'L0_rec_rv2': (1.0, 0.6)}
    factors = {'L0_rec_rw1': 2.73}
    for name, (base, spread) in spreads.items():
        noise = np.random.default_rng([zlib.crc32(name.encode()), seed]).standard_normal(out[name].shape)
        drawn = base * np.exp(spread * noise) if base else spread * noise
        out[name] = jnp.asarray(drawn.astype(out[name].dtype))
    for name, factor in factors.items():
        out[name] = (out[name] * factor).astype(out[name].dtype)
    return out
```

```python
from contextlib import ExitStack

import concourse.bass as bass
from concourse import mybir

ALU = mybir.AluOpType
ACT = mybir.ActivationFunctionType
F32 = mybir.dt.float32
F32R = mybir.dt.float32r
I32 = mybir.dt.int32

P = 128
B, N, C = 4096, 48, 48
HD1, HD2, BLOCKS = 512, 256, 2
EPS = 1e-5
TB = 512
TILES = B // TB

NG, CG = 8, 16
GROUPS, CGROUPS = N // NG, C // CG
CHUNKS = GROUPS * CGROUPS
M1, M2 = HD1 // P, HD2 // P
SLOTS = 9
CHUNKS_PER_STAGE = 3
assert CHUNKS % SLOTS == 0

BN_COLS = M1 + M2 + BLOCKS * 2 * M2
BN_FC1, BN_FC2 = 0, M1
V_B, V_G, V_BE, V_M, V_V = range(5)
DENSE_CHUNKS = M1 + BLOCKS * 2 * M2


def bn_res(i, half):
    return M1 + M2 + (2 * i + half) * M2


def w_res(i, half):
    return M1 + (2 * i + half) * M2


def mlp_kernel(nc, z_t, w1_t, dense_t, bn_vectors, wout_t, bout, categories, y):
    with ExitStack() as ctx:
        def sb(name, shape, dt=F32):
            return ctx.enter_context(nc.sbuf_tensor(name, shape, dt))

        def psum(name):
            return ctx.enter_context(nc.psum_tensor(name, [P, TB], F32))

        def sem(name):
            return ctx.enter_context(nc.semaphore(name))

        w1_raw = sb("w1_raw", [P, CHUNKS, HD1])
        w1_hi = sb("w1_hi", [P, CHUNKS, HD1], F32R)
        w1_lo = sb("w1_lo", [P, CHUNKS, HD1], F32R)
        dense_w = sb("dense_w", [P, DENSE_CHUNKS, HD2])
        ones = sb("ones", [P, 1])
        cats = sb("cats", [P, CGROUPS])
        vectors = sb("vectors", [P, 5, BN_COLS])
        wout = sb("wout", [P, M2])
        bout_sb = sb("bout_sb", [1, 1])
        bn_scale = sb("bn_scale", [P, BN_COLS])
        bn_shift = sb("bn_shift", [P, BN_COLS])
        bn_tmp = sb("bn_tmp", [P, 4, BN_COLS])

        z_bc = sb("z_bc", [P, GROUPS, TB], I32)
        onehot = sb("onehot", [P, SLOTS, TB], F32R)
        h1 = sb("h1", [P, M1, TB])
        x = [sb(f"x{i}", [P, M2, TB]) for i in range(BLOCKS + 1)]
        hid = [sb(f"hid{i}", [P, M2, TB]) for i in range(BLOCKS)]
        presum = [sb(f"presum{i}", [P, M2, TB]) for i in range(BLOCKS)]
        weighted = sb("weighted", [P, 2, TB])
        y_row = sb("y_row", [1, TB])

        fc1_ps = [psum(f"fc1_ps{m}") for m in range(M1)]
        even_ps = [psum(f"even_ps{m}") for m in range(M2)]
        odd_ps = [psum(f"odd_ps{m}") for m in range(M2)]

        z_in = [sem(f"z_in{g}") for g in range(GROUPS)]
        w1_in = [sem(f"w1_in{k}") for k in range(CHUNKS)]
        small_in = sem("small_in")
        cats_in = sem("cats_in")
        dense_in = sem("dense_in")
        w1_hi_ready = sem("w1_hi_ready")
        w1_lo_ready = sem("w1_lo_ready")
        sqrt_ready = sem("sqrt_ready")
        bn_step = sem("bn_step")
        bn_ready = sem("bn_ready")
        onehot_ready = sem("onehot_ready")
        onehot_used = sem("onehot_used")
        fc1_summed = sem("fc1_summed")
        h1_ready = sem("h1_ready")
        fc2_summed = sem("fc2_summed")
        x_ready = [sem(f"x{i}_ready") for i in range(BLOCKS + 1)]
        first_summed = [sem(f"first_summed{i}") for i in range(BLOCKS)]
        hid_ready = [sem(f"hid{i}_ready") for i in range(BLOCKS)]
        second_summed = [sem(f"second_summed{i}") for i in range(BLOCKS)]
        presum_ready = [sem(f"presum{i}_ready") for i in range(BLOCKS)]
        weighted_step = sem("weighted_step")
        weighted_ready = sem("weighted_ready")
        y_summed = sem("y_summed")
        y_ready = sem("y_ready")
        y_stored = sem("y_stored")

        def z_rows(g, t):
            rows = z_t[g * NG:(g + 1) * NG, bass.ts(t, TB)]
            return rows.partition_broadcast(CG)

        block = ctx.enter_context(nc.Block())

        @block.sync
        def _(sp):
            def load_z(g, t):
                sp.dma_start(z_bc[:, g, :], z_rows(g, t)).then_inc(z_in[g], 16)

            def reload_z(t):
                for g in range(GROUPS):
                    sp.wait_ge(onehot_ready, CHUNKS * (t - 1) + CGROUPS * (g + 1))
                    load_z(g, t)

            def store_y(t):
                sp.wait_ge(y_ready, t + 1)
                sp.dma_start(y[:, bass.ts(t, TB)], y_row[:, :]).then_inc(y_stored, 16)

            sp.dma_start(cats[:, :], categories).then_inc(cats_in, 16)
            for g in range(GROUPS):
                load_z(g, 0)
                for k in range(CGROUPS * g, CGROUPS * (g + 1)):
                    sp.dma_start(w1_raw[:, k, :], w1_t[k]).then_inc(w1_in[k], 16)
            sp.dma_start(vectors[:, :, :], bn_vectors).then_inc(small_in, 16)
            sp.dma_start(wout[:, :], wout_t).then_inc(small_in, 16)
            sp.dma_start(bout_sb[:, :], bout).then_inc(small_in, 16)
            sp.dma_start(dense_w[:, :, :], dense_t).then_inc(dense_in, 16)
            reload_z(1)
            with sp.Fori(2, TILES) as t:
                reload_z(t)
                store_y(t - 2)
            store_y(TILES - 2)
            store_y(TILES - 1)
            sp.wait_ge(y_stored, 16 * TILES)

        @block.tensor
        def _(pe):
            def fc1_chunk(t, k):
                pe.wait_ge(onehot_ready, CHUNKS * t + k + 1)
                for m in range(M1):
                    if k == 0 and not (isinstance(t, int) and t == 0):
                        pe.wait_ge(h1_ready, M1 * (t - 1) + m + 1)
                    cols = slice(m * P, (m + 1) * P)
                    nc.tensor.matmul(fc1_ps[m][:, :], w1_hi[:, k, cols], onehot[:, k % SLOTS, :],
                                     start=(k == 0), stop=False)
                    last = nc.tensor.matmul(fc1_ps[m][:, :], w1_lo[:, k, cols],
                                            onehot[:, k % SLOTS, :],
                                            start=False, stop=(k == CHUNKS - 1))
                    if k == CHUNKS - 1 and m < M1 - 1:
                        last.then_inc(fc1_summed, 1)
                if k == CHUNKS - 1:
                    last.then_inc(fc1_summed, 1)
                else:
                    last.then_inc(onehot_used, 1)

            def small_layer(out_ps, w_chunk, src, k_chunks, summed):
                for m in range(M2):
                    for k in range(k_chunks):
                        last = nc.tensor.matmul(out_ps[m][:, :],
                                                dense_w[:, w_chunk + k, m * P:(m + 1) * P],
                                                src[:, k, :], start=(k == 0),
                                                stop=(k == k_chunks - 1))
                    last.then_inc(summed, 1)

            def stage(s, t):
                if s == 0:
                    pe.wait_ge(h1_ready, M1 * (t + 1))
                    small_layer(even_ps, 0, h1, M1, fc2_summed)
                elif s <= 2 * BLOCKS:
                    i, half = divmod(s - 1, 2)
                    if half == 0:
                        pe.wait_ge(x_ready[i], M2 * (t + 1))
                        if i == 0 and not (isinstance(t, int) and t == 0):
                            pe.wait_ge(y_ready, t)
                        small_layer(odd_ps, w_res(i, 0), x[i], M2, first_summed[i])
                    else:
                        pe.wait_ge(hid_ready[i], M2 * (t + 1))
                        small_layer(even_ps, w_res(i, 1), hid[i], M2, second_summed[i])
                else:
                    pe.wait_ge(weighted_ready, t + 1)
                    nc.tensor.matmul(odd_ps[0][0:1, :], ones[:, 0:1], weighted[:, 1, :],
                                     start=True, stop=True).then_inc(y_summed, 1)

            def tile_step(t):
                for k in range(CHUNKS):
                    fc1_chunk(t, k)
                    if (k + 1) % CHUNKS_PER_STAGE == 0:
                        stage((k + 1) // CHUNKS_PER_STAGE - 1, t - 1)

            for k in range(CHUNKS):
                pe.wait_ge(w1_lo_ready, k + 1)
                fc1_chunk(0, k)
            pe.wait_ge(dense_in, 16)
            with pe.Fori(1, TILES) as t:
                tile_step(t)
            for s in range(2 * BLOCKS + 2):
                stage(s, TILES - 1)

        @block.scalar
        def _(act):
            def norm_relu(out, sums, col):
                return nc.scalar.activation(out, sums, ACT.Relu, bias=bn_shift[:, col:col + 1],
                                            scale=bn_scale[:, col:col + 1])

            def evacuate_fc1(t):
                for m in range(M1):
                    act.wait_ge(fc1_summed, M1 * t + m + 1)
                    norm_relu(h1[:, m, :], fc1_ps[m][:, :], BN_FC1 + m).then_inc(h1_ready, 1)

            def small_layers(t):
                for m in range(M2):
                    act.wait_ge(fc2_summed, M2 * t + m + 1)
                    norm_relu(x[0][:, m, :], even_ps[m][:, :], BN_FC2 + m).then_inc(x_ready[0], 1)
                for i in range(BLOCKS):
                    for m in range(M2):
                        act.wait_ge(first_summed[i], M2 * t + m + 1)
                        norm_relu(hid[i][:, m, :], odd_ps[m][:, :],
                                  bn_res(i, 0) + m).then_inc(hid_ready[i], 1)
                    for m in range(M2):
                        act.wait_ge(presum_ready[i], M2 * t + m + 1)
                        col = bn_res(i, 1) + m
                        nc.scalar.activation(x[i + 1][:, m, :], presum[i][:, m, :], ACT.Relu,
                                             bias=bn_shift[:, col:col + 1]
                                             ).then_inc(x_ready[i + 1], 1)

            def finish_y(t):
                act.wait_ge(y_summed, t + 1)
                if not (isinstance(t, int) and t == 0):
                    act.wait_ge(y_stored, 16 * t)
                nc.scalar.activation(y_row[:, :], odd_ps[0][0:1, :], ACT.Identity,
                                     bias=bout_sb[:, 0:1]).then_inc(y_ready, 1)

            for k in range(CHUNKS):
                act.wait_ge(w1_in[k], 16)
                nc.scalar.activation(w1_hi[:, k, :], w1_raw[:, k, :],
                                     ACT.Copy).then_inc(w1_hi_ready, 1)
            act.wait_ge(bn_step, 1)
            nc.scalar.activation(bn_tmp[:, 1, :], bn_tmp[:, 0, :], ACT.Sqrt).then_inc(sqrt_ready, 1)
            act.wait_ge(bn_ready, 1)
            evacuate_fc1(0)
            with act.Fori(1, TILES) as t:
                small_layers(t - 1)
                evacuate_fc1(t)
                finish_y(t - 1)
            small_layers(TILES - 1)
            finish_y(TILES - 1)

        @block.vector
        def _(dve):
            def make_onehot(t, k):
                g, cg = divmod(k, CGROUPS)
                if cg == 0:
                    dve.wait_ge(z_in[g], 16 * (t + 1))
                first = isinstance(t, int) and t == 0
                if not (first and k < SLOTS):
                    if k < SLOTS - 1 or k >= SLOTS:
                        before = (CHUNKS - 1) * t + k - SLOTS + 1 if k >= SLOTS else \
                            (CHUNKS - 1) * (t - 1) + CHUNKS + k - SLOTS + 1
                        dve.wait_ge(onehot_used, before)
                    else:
                        dve.wait_ge(fc1_summed, M1 * t)
                made = nc.vector.tensor_scalar(onehot[:, k % SLOTS, :], z_bc[:, g, :],
                                               cats[:, cg:cg + 1], None, ALU.is_equal)
                made.then_inc(onehot_ready, 1)

            def split_lo(k):
                dve.wait_ge(w1_in[k], 16)
                dve.wait_ge(w1_hi_ready, k + 1)
                nc.vector.tensor_tensor(w1_lo[:, k, :], w1_raw[:, k, :],
                                        w1_hi[:, k, :].bitcast(F32),
                                        ALU.subtract).then_inc(w1_lo_ready, 1)

            def add_residual(i, t):
                for m in range(M2):
                    dve.wait_ge(second_summed[i], M2 * t + m + 1)
                    col = bn_res(i, 1) + m
                    nc.vector.scalar_tensor_tensor(presum[i][:, m, :], even_ps[m][:, :],
                                                   bn_scale[:, col:col + 1], x[i][:, m, :],
                                                   ALU.mult, ALU.add).then_inc(presum_ready[i], 1)

            def weigh_output(t):
                dve.wait_ge(x_ready[BLOCKS], M2 * t + 1)
                nc.vector.tensor_scalar(weighted[:, 0, :], x[BLOCKS][:, 0, :], wout[:, 0:1], None,
                                        ALU.mult).then_inc(weighted_step, 1)
                dve.wait_ge(x_ready[BLOCKS], M2 * t + 2)
                dve.wait_ge(weighted_step, t + 1)
                nc.vector.scalar_tensor_tensor(weighted[:, 1, :], x[BLOCKS][:, 1, :], wout[:, 1:2],
                                               weighted[:, 0, :], ALU.mult,
                                               ALU.add).then_inc(weighted_ready, 1)

            def fold_batch_norm():
                steps = [0]

                def done(ins):
                    steps[0] += 1
                    ins.then_inc(bn_step, 1)
                    dve.wait_ge(bn_step, steps[0])

                var, root, inv, t3 = (bn_tmp[:, i, :] for i in range(4))
                dve.wait_ge(small_in, 48)
                done(nc.vector.tensor_scalar(var, vectors[:, V_V, :], EPS, None, ALU.add))
                dve.wait_ge(sqrt_ready, 1)
                done(nc.vector.reciprocal(inv, root))
                done(nc.vector.tensor_tensor(t3, inv, inv, ALU.mult))
                done(nc.vector.tensor_tensor(t3, t3, var, ALU.mult))
                done(nc.vector.tensor_scalar(t3, t3, -0.5, 1.5, ALU.mult, ALU.add))
                done(nc.vector.tensor_tensor(inv, inv, t3, ALU.mult))
                done(nc.vector.tensor_tensor(bn_scale[:, :], vectors[:, V_G, :], inv, ALU.mult))
                done(nc.vector.tensor_tensor(t3, vectors[:, V_B, :], vectors[:, V_M, :],
                                             ALU.subtract))
                done(nc.vector.tensor_tensor(t3, t3, bn_scale[:, :], ALU.mult))
                nc.vector.tensor_tensor(bn_shift[:, :], t3, vectors[:, V_BE, :],
                                        ALU.add).then_inc(bn_ready, 1)

            def tile_step(t):
                for k in range(CHUNKS):
                    make_onehot(t, k)
                for i in range(BLOCKS):
                    add_residual(i, t - 1)
                weigh_output(t - 1)

            nc.vector.memset(ones[:, :], 1.0)
            dve.wait_ge(cats_in, 16)
            for k in range(CHUNKS):
                if k == SLOTS:
                    fold_batch_norm()
                make_onehot(0, k)
                split_lo(k)
            with dve.Fori(1, TILES) as t:
                tile_step(t)
            for i in range(BLOCKS):
                add_residual(i, TILES - 1)
            weigh_output(TILES - 1)


def kernel(**inputs):
    import numpy as np
    import concourse.bacc as bacc
    from concourse.bass_utils import run_bass_kernel_spmd

    def get(name):
        return np.asarray(inputs["L0_rec_" + name])

    def columns(v):
        return v.reshape(-1, P).T

    def per_feature(name):
        parts = [columns(get(name + "1")), columns(get(name + "2"))]
        for i in range(BLOCKS):
            parts += [columns(get("r" + name + "1")[i]), columns(get("r" + name + "2")[i])]
        return np.concatenate(parts, axis=1)

    w1 = get("w1").T.reshape(GROUPS, NG, CGROUPS, CG, HD1).transpose(0, 2, 3, 1, 4)
    dense = [get("w2").T.reshape(M1, P, HD2)]
    for i in range(BLOCKS):
        dense += [get("rw1")[i].T.reshape(M2, P, HD2), get("rw2")[i].T.reshape(M2, P, HD2)]
    partition = np.arange(P)[:, None]
    arrays = {
        "z_t": np.asarray(inputs["r_z"]).T,
        "w1_t": w1.reshape(CHUNKS, P, HD1),
        "dense_t": np.concatenate(dense, axis=0).transpose(1, 0, 2),
        "bn_vectors": np.stack([per_feature(n) for n in ("b", "g", "be", "m", "v")], axis=1),
        "wout_t": columns(get("wout").reshape(-1)),
        "bout": get("bout").reshape(1, 1),
        "categories": (partition // NG + CG * np.arange(CGROUPS)[None, :]).astype(np.float32),
    }
    arrays = {name: np.ascontiguousarray(a) for name, a in arrays.items()}

    nc = bacc.Bacc("TRN2", target_bir_lowering=False, num_devices=1)
    args = [nc.dram_tensor(name, a.shape, mybir.dt.from_np(a.dtype), kind="ExternalInput").ap()
            for name, a in arrays.items()]
    out = nc.dram_tensor("y", (1, B), F32, kind="ExternalOutput").ap()
    mlp_kernel(nc, *args, out)
    r = run_bass_kernel_spmd(nc, [arrays], core_ids=[0])
    return r.results[0]["y"].reshape(-1)
```

```python
from contextlib import ExitStack

import concourse.bass as bass
from concourse import mybir

ALU = mybir.AluOpType
ACT = mybir.ActivationFunctionType
F32 = mybir.dt.float32
F32R = mybir.dt.float32r
I32 = mybir.dt.int32

P = 128
B, N, C = 4096, 48, 48
HD1, HD2, BLOCKS = 512, 256, 2
EPS = 1e-5
TB = 512
TILES = B // TB

NG, CG = 8, 16
GROUPS, CGROUPS = N // NG, C // CG
CHUNKS = GROUPS * CGROUPS
M1, M2 = HD1 // P, HD2 // P
SLOTS = 9
CHUNKS_PER_STAGE = 3
TAIL_START = CHUNKS - CHUNKS_PER_STAGE
LAST_PARTS = 2
WARM_UP = 8
assert CHUNKS % SLOTS == 0 and M1 == 2 * M2

BN_COLS = M1 + M2 + BLOCKS * 2 * M2
BN_FC1, BN_FC2 = 0, M1
V_B, V_G, V_BE, V_M, V_V = range(5)
DENSE_CHUNKS = M1 + BLOCKS * 2 * M2


def bn_res(i, half):
    return M1 + M2 + (2 * i + half) * M2


def w_res(i, half):
    return M1 + (2 * i + half) * M2


def mlp_kernel(nc, z_t, w1_t, dense_t, bn_vectors, wout_t, bout, categories, y):
    with ExitStack() as ctx:
        def sb(name, shape, dt=F32):
            return ctx.enter_context(nc.sbuf_tensor(name, shape, dt))

        def psum(name):
            return ctx.enter_context(nc.psum_tensor(name, [P, TB], F32))

        def sem(name):
            return ctx.enter_context(nc.semaphore(name))

        w1_raw = sb("w1_raw", [P, CHUNKS, HD1])
        w1_hi = sb("w1_hi", [P, CHUNKS, HD1], F32R)
        w1_lo = sb("w1_lo", [P, CHUNKS, HD1], F32R)
        dense_w = sb("dense_w", [P, DENSE_CHUNKS, HD2])
        ones = sb("ones", [P, P], F32R)
        cats = sb("cats", [P, CGROUPS])
        vectors = sb("vectors", [P, 5, BN_COLS])
        wout = sb("wout", [P, M2])
        bout_sb = sb("bout_sb", [1, 1])
        bn_scale = sb("bn_scale", [P, BN_COLS])
        bn_shift = sb("bn_shift", [P, BN_COLS])
        bn_tmp = sb("bn_tmp", [P, 4, BN_COLS])
        warm = sb("warm", [P, TB], mybir.dt.bfloat16)

        z_bc = sb("z_bc", [P, GROUPS, TB], I32)
        onehot = sb("onehot", [P, SLOTS, TB], F32R)
        h1 = sb("h1", [P, M1, TB])
        x = [sb(f"x{i}", [P, M2, TB]) for i in range(BLOCKS + 1)]
        hid = [sb(f"hid{i}", [P, M2, TB]) for i in range(BLOCKS)]
        presum = [sb(f"presum{i}", [P, M2, TB]) for i in range(BLOCKS)]
        weighted = sb("weighted", [P, 2, TB])
        weighted_hi = sb("weighted_hi", [P, TB], F32R)
        weighted_lo = sb("weighted_lo", [P, TB], F32R)
        y_row = sb("y_row", [1, TB])

        fc1_ps = [psum(f"fc1_ps{m}") for m in range(M1)]
        even_ps = [psum(f"even_ps{m}") for m in range(M2)]
        odd_ps = [psum(f"odd_ps{m}") for m in range(M2)]

        z_in = [sem(f"z_in{g}") for g in range(GROUPS)]
        w1_in = [sem(f"w1_in{k}") for k in range(CHUNKS)]
        vectors_in = sem("vectors_in")
        wout_in = sem("wout_in")
        bout_in = sem("bout_in")
        cats_in = sem("cats_in")
        dense_in = sem("dense_in")
        warm_set = sem("warm_set")
        ones_set = sem("ones_set")
        w1_hi_ready = sem("w1_hi_ready")
        w1_lo_ready = sem("w1_lo_ready")
        sqrt_ready = sem("sqrt_ready")
        bn_step = sem("bn_step")
        bn_ready = sem("bn_ready")
        onehot_ready = sem("onehot_ready")
        onehot_used = sem("onehot_used")
        fc1_summed = sem("fc1_summed")
        h1_ready = sem("h1_ready")
        fc2_summed = sem("fc2_summed")
        x_ready = [sem(f"x{i}_ready") for i in range(BLOCKS + 1)]
        first_summed = [sem(f"first_summed{i}") for i in range(BLOCKS)]
        hid_ready = [sem(f"hid{i}_ready") for i in range(BLOCKS)]
        second_summed = [sem(f"second_summed{i}") for i in range(BLOCKS)]
        presum_ready = [sem(f"presum{i}_ready") for i in range(BLOCKS)]
        weighted_first = sem("weighted_first")
        weighted_ready = sem("weighted_ready")
        weighted_hi_ready = sem("weighted_hi_ready")
        weighted_lo_ready = sem("weighted_lo_ready")
        y_summed = sem("y_summed")
        y_ready = sem("y_ready")
        y_stored = sem("y_stored")
        y_row_free = sem("y_row_free")

        whole = (slice(0, TB), even_ps, odd_ps)
        half = TB // LAST_PARTS
        last_parts = [(slice(0, half), even_ps, odd_ps),
                      (slice(half, TB), fc1_ps[:M2], fc1_ps[M2:])]

        def is_first(n):
            return isinstance(n, int) and n == 0

        block = ctx.enter_context(nc.Block())

        @block.sync
        def _(sp):
            def load_z(g, t):
                rows = z_t[g * NG:(g + 1) * NG, bass.ts(t, TB)]
                sp.dma_start(z_bc[:, g, :], rows.partition_broadcast(CG)).then_inc(z_in[g], 16)

            def reload_z(t):
                for g in range(GROUPS):
                    sp.wait_ge(onehot_ready, CHUNKS * (t - 1) + CGROUPS * (g + 1))
                    load_z(g, t)

            def store_y(t):
                sp.wait_ge(y_ready, t + 1)
                sp.dma_start(y[:, bass.ts(t, TB)], y_row[:, :]).then_inc(y_stored, 16)
                sp.wait_ge(y_stored, 16 * (t + 1))
                sp.sem_inc(y_row_free, 1)

            sp.sem_inc(y_row_free, 1)
            load_z(0, 0)
            for k in range(1, CGROUPS):
                sp.dma_start(w1_raw[:, k, :], w1_t[k]).then_inc(w1_in[k], 16)
            sp.dma_start(vectors[:, :, :], bn_vectors).then_inc(vectors_in, 16)
            sp.dma_start(wout[:, :], wout_t).then_inc(wout_in, 16)
            sp.dma_start(bout_sb[:, :], bout).then_inc(bout_in, 16)
            for g in range(1, GROUPS):
                load_z(g, 0)
                for k in range(CGROUPS * g, CGROUPS * (g + 1)):
                    sp.dma_start(w1_raw[:, k, :], w1_t[k]).then_inc(w1_in[k], 16)
            sp.dma_start(dense_w[:, :, :], dense_t).then_inc(dense_in, 16)
            reload_z(1)
            with sp.Fori(2, TILES) as t:
                reload_z(t)
                store_y(t - 2)
            store_y(TILES - 2)
            last = TILES - 1
            for part, (cols, _, _) in enumerate(last_parts):
                sp.wait_ge(y_ready, last + part + 1)
                sp.dma_start(y[:, last * TB + cols.start:last * TB + cols.stop],
                             y_row[:, cols]).then_inc(y_stored, 16)
            sp.wait_ge(y_stored, 16 * (last + LAST_PARTS))

        @block.gpsimd
        def _(pool):
            pool.dma_start(cats[:, :], categories).then_inc(cats_in, 16)
            nc.gpsimd.memset(warm[:, :], 0.0).then_inc(warm_set, 1)

        @block.tensor
        def _(pe):
            def fc1_product(m, k):
                cols = slice(m * P, (m + 1) * P)
                nc.tensor.matmul(fc1_ps[m][:, :], w1_hi[:, k, cols], onehot[:, k % SLOTS, :],
                                 start=(k == 0), stop=False)
                return nc.tensor.matmul(fc1_ps[m][:, :], w1_lo[:, k, cols],
                                        onehot[:, k % SLOTS, :], start=False,
                                        stop=(k == CHUNKS - 1))

            def fc1_chunk(t, k):
                pe.wait_ge(onehot_ready, CHUNKS * t + k + 1)
                for m in range(M1):
                    if k == 0 and not is_first(t):
                        pe.wait_ge(h1_ready, M1 * (t - 1) + m + 1)
                    last = fc1_product(m, k)
                last.then_inc(onehot_used, 1)

            def fc1_last_chunks(t):
                pe.wait_ge(onehot_ready, CHUNKS * (t + 1))
                for m in range(M1):
                    for k in range(TAIL_START, CHUNKS):
                        last = fc1_product(m, k)
                    last.then_inc(fc1_summed, 1)

            def small_layer(out_ps, cols, w_chunk, src, k_chunks, src_ready, before, summed):
                for k in range(k_chunks):
                    pe.wait_ge(src_ready, before + k + 1)
                    for m in range(M2):
                        last = nc.tensor.matmul(out_ps[m][:, cols],
                                                dense_w[:, w_chunk + k, m * P:(m + 1) * P],
                                                src[:, k, cols], start=(k == 0),
                                                stop=(k == k_chunks - 1))
                        if k == k_chunks - 1:
                            last.then_inc(summed, 1)

            def fc2(t, part):
                cols, even, _ = part
                small_layer(even, cols, 0, h1, M1, h1_ready, M1 * t, fc2_summed)

            def block_layer(s, n, part):
                cols, even, odd = part
                i, second = divmod(s, 2)
                if second:
                    small_layer(even, cols, w_res(i, 1), hid[i], M2, hid_ready[i], M2 * n,
                                second_summed[i])
                else:
                    small_layer(odd, cols, w_res(i, 0), x[i], M2, x_ready[i], M2 * n,
                                first_summed[i])

            def sum_y(t):
                pe.wait_ge(weighted_hi_ready, t + 1)
                nc.tensor.matmul(odd_ps[0][:, :], ones[:, :], weighted_hi[:, :],
                                 start=True, stop=False)
                pe.wait_ge(weighted_lo_ready, t + 1)
                nc.tensor.matmul(odd_ps[0][:, :], ones[:, :], weighted_lo[:, :],
                                 start=False, stop=True).then_inc(y_summed, 1)

            def stage(s, t):
                if s == 0:
                    fc2(t, whole)
                elif s <= 2 * BLOCKS:
                    block_layer(s - 1, t, whole)
                else:
                    sum_y(t)

            def tile_step(t):
                for k in range(TAIL_START):
                    fc1_chunk(t, k)
                    if (k + 1) % CHUNKS_PER_STAGE == 0:
                        stage((k + 1) // CHUNKS_PER_STAGE - 1, t - 1)
                fc1_last_chunks(t)
                stage(2 * BLOCKS + 1, t - 1)

            pe.wait_ge(warm_set, 1)
            for _ in range(WARM_UP):
                nc.tensor.matmul(odd_ps[1][:, :], warm[:, 0:P], warm[:, :], start=True, stop=True)
            for k in range(TAIL_START):
                pe.wait_ge(w1_lo_ready, k + 1)
                fc1_chunk(0, k)
            pe.wait_ge(w1_lo_ready, CHUNKS)
            fc1_last_chunks(0)
            pe.wait_ge(dense_in, 16)
            pe.wait_ge(ones_set, 1)
            with pe.Fori(1, TILES) as t:
                tile_step(t)

            last = TILES - 1
            for part in last_parts:
                fc2(last, part)
            for s in range(2 * BLOCKS):
                for n, part in enumerate(last_parts):
                    block_layer(s, last + n, part)
            for n, (cols, _, odd) in enumerate(last_parts):
                for m in range(M2):
                    pe.wait_ge(x_ready[BLOCKS], M2 * (last + n) + m + 1)
                    end = nc.tensor.matmul(odd[0][0:1, cols], wout[:, m:m + 1],
                                           x[BLOCKS][:, m, cols], start=(m == 0),
                                           stop=(m == M2 - 1))
                end.then_inc(y_summed, 1)

        @block.scalar
        def _(act):
            def norm_relu(out, sums, col):
                return nc.scalar.activation(out, sums, ACT.Relu, bias=bn_shift[:, col:col + 1],
                                            scale=bn_scale[:, col:col + 1])

            def evacuate_fc1(t):
                for m in range(M1):
                    act.wait_ge(fc1_summed, M1 * t + m + 1)
                    norm_relu(h1[:, m, :], fc1_ps[m][:, :], BN_FC1 + m).then_inc(h1_ready, 1)

            def after_fc2(n, part):
                cols, even, _ = part
                for m in range(M2):
                    act.wait_ge(fc2_summed, M2 * n + m + 1)
                    norm_relu(x[0][:, m, cols], even[m][:, cols],
                              BN_FC2 + m).then_inc(x_ready[0], 1)

            def after_first(i, n, part):
                cols, _, odd = part
                for m in range(M2):
                    act.wait_ge(first_summed[i], M2 * n + m + 1)
                    norm_relu(hid[i][:, m, cols], odd[m][:, cols],
                              bn_res(i, 0) + m).then_inc(hid_ready[i], 1)

            def after_second(i, n, part):
                cols = part[0]
                for m in range(M2):
                    act.wait_ge(presum_ready[i], M2 * n + m + 1)
                    col = bn_res(i, 1) + m
                    nc.scalar.activation(x[i + 1][:, m, cols], presum[i][:, m, cols], ACT.Relu,
                                         bias=bn_shift[:, col:col + 1]
                                         ).then_inc(x_ready[i + 1], 1)

            def finish_y(n, cols, odd):
                act.wait_ge(y_summed, n + 1)
                nc.scalar.activation(y_row[:, cols], odd[0][0:1, cols], ACT.Identity,
                                     bias=bout_sb[:, 0:1]).then_inc(y_ready, 1)

            act.dma_start(w1_raw[:, 0, :], w1_t[0]).then_inc(w1_in[0], 16)
            for k in range(CHUNKS):
                act.wait_ge(w1_in[k], 16)
                nc.scalar.activation(w1_hi[:, k, :], w1_raw[:, k, :],
                                     ACT.Copy).then_inc(w1_hi_ready, 1)
            act.wait_ge(bn_step, 1)
            nc.scalar.activation(bn_tmp[:, 1, :], bn_tmp[:, 0, :], ACT.Sqrt).then_inc(sqrt_ready, 1)
            act.wait_ge(bn_ready, 1)
            act.wait_ge(bout_in, 16)
            evacuate_fc1(0)
            with act.Fori(1, TILES) as t:
                after_fc2(t - 1, whole)
                for i in range(BLOCKS):
                    after_first(i, t - 1, whole)
                    after_second(i, t - 1, whole)
                act.wait_ge(weighted_ready, t)
                nc.scalar.activation(weighted_hi[:, :], weighted[:, 1, :],
                                     ACT.Copy).then_inc(weighted_hi_ready, 1)
                evacuate_fc1(t)
                act.wait_ge(y_row_free, t)
                finish_y(t - 1, slice(0, TB), odd_ps)
            last = TILES - 1
            for n, part in enumerate(last_parts):
                after_fc2(last + n, part)
            for i in range(BLOCKS):
                for n, part in enumerate(last_parts):
                    after_first(i, last + n, part)
                for n, part in enumerate(last_parts):
                    after_second(i, last + n, part)
            act.wait_ge(y_row_free, TILES)
            for n, (cols, _, odd) in enumerate(last_parts):
                finish_y(last + n, cols, odd)

        @block.vector
        def _(dve):
            def make_onehot(t, k):
                g, cg = divmod(k, CGROUPS)
                if cg == 0:
                    dve.wait_ge(z_in[g], 16 * (t + 1))
                if not (is_first(t) and k < SLOTS):
                    if k >= SLOTS:
                        dve.wait_ge(onehot_used, TAIL_START * t + k - SLOTS + 1)
                    elif k + SLOTS < TAIL_START:
                        dve.wait_ge(onehot_used, TAIL_START * (t - 1) + k + SLOTS + 1)
                    else:
                        dve.wait_ge(fc1_summed, M1 * t)
                nc.vector.tensor_scalar(onehot[:, k % SLOTS, :], z_bc[:, g, :],
                                        cats[:, cg:cg + 1], None,
                                        ALU.is_equal).then_inc(onehot_ready, 1)

            def split_lo(k):
                dve.wait_ge(w1_in[k], 16)
                dve.wait_ge(w1_hi_ready, k + 1)
                nc.vector.tensor_tensor(w1_lo[:, k, :], w1_raw[:, k, :],
                                        w1_hi[:, k, :].bitcast(F32),
                                        ALU.subtract).then_inc(w1_lo_ready, 1)

            def add_residual(i, n, part):
                cols, even, _ = part
                for m in range(M2):
                    dve.wait_ge(second_summed[i], M2 * n + m + 1)
                    col = bn_res(i, 1) + m
                    nc.vector.scalar_tensor_tensor(presum[i][:, m, cols], even[m][:, cols],
                                                   bn_scale[:, col:col + 1], x[i][:, m, cols],
                                                   ALU.mult, ALU.add).then_inc(presum_ready[i], 1)

            def weigh_output(t):
                dve.wait_ge(x_ready[BLOCKS], M2 * t + 1)
                nc.vector.tensor_scalar(weighted[:, 0, :], x[BLOCKS][:, 0, :], wout[:, 0:1], None,
                                        ALU.mult).then_inc(weighted_first, 1)
                dve.wait_ge(x_ready[BLOCKS], M2 * t + 2)
                dve.wait_ge(weighted_first, t + 1)
                nc.vector.scalar_tensor_tensor(weighted[:, 1, :], x[BLOCKS][:, 1, :], wout[:, 1:2],
                                               weighted[:, 0, :], ALU.mult,
                                               ALU.add).then_inc(weighted_ready, 1)
                dve.wait_ge(weighted_hi_ready, t + 1)
                nc.vector.tensor_tensor(weighted_lo[:, :], weighted[:, 1, :],
                                        weighted_hi[:, :].bitcast(F32),
                                        ALU.subtract).then_inc(weighted_lo_ready, 1)

            def fold_batch_norm():
                steps = [0]

                def done(ins):
                    steps[0] += 1
                    ins.then_inc(bn_step, 1)
                    dve.wait_ge(bn_step, steps[0])

                var, root, inv, t3 = (bn_tmp[:, i, :] for i in range(4))
                dve.wait_ge(vectors_in, 16)
                done(nc.vector.tensor_scalar(var, vectors[:, V_V, :], EPS, None, ALU.add))
                dve.wait_ge(sqrt_ready, 1)
                done(nc.vector.reciprocal(inv, root))
                done(nc.vector.tensor_tensor(t3, inv, inv, ALU.mult))
                done(nc.vector.tensor_tensor(t3, t3, var, ALU.mult))
                done(nc.vector.tensor_scalar(t3, t3, -0.5, 1.5, ALU.mult, ALU.add))
                done(nc.vector.tensor_tensor(inv, inv, t3, ALU.mult))
                done(nc.vector.tensor_tensor(bn_scale[:, :], vectors[:, V_G, :], inv, ALU.mult))
                done(nc.vector.tensor_tensor(t3, vectors[:, V_B, :], vectors[:, V_M, :],
                                             ALU.subtract))
                done(nc.vector.tensor_tensor(t3, t3, bn_scale[:, :], ALU.mult))
                nc.vector.tensor_tensor(bn_shift[:, :], t3, vectors[:, V_BE, :],
                                        ALU.add).then_inc(bn_ready, 1)

            dve.wait_ge(cats_in, 16)
            for k in range(CHUNKS):
                make_onehot(0, k)
                split_lo(k)
            nc.vector.memset(ones[:, :].bitcast(F32), 1.0).then_inc(ones_set, 1)
            fold_batch_norm()
            dve.wait_ge(wout_in, 16)
            with dve.Fori(1, TILES) as t:
                for k in range(CHUNKS):
                    make_onehot(t, k)
                for i in range(BLOCKS):
                    add_residual(i, t - 1, whole)
                weigh_output(t - 1)
            for i in range(BLOCKS):
                for n, part in enumerate(last_parts):
                    add_residual(i, TILES - 1 + n, part)


def kernel(**inputs):
    import numpy as np
    import concourse.bacc as bacc
    from concourse.bass_utils import run_bass_kernel_spmd

    def get(name):
        return np.asarray(inputs["L0_rec_" + name])

    def columns(v):
        return v.reshape(-1, P).T

    def per_feature(name):
        parts = [columns(get(name + "1")), columns(get(name + "2"))]
        for i in range(BLOCKS):
            parts += [columns(get("r" + name + "1")[i]), columns(get("r" + name + "2")[i])]
        return np.concatenate(parts, axis=1)

    w1 = get("w1").T.reshape(GROUPS, NG, CGROUPS, CG, HD1).transpose(0, 2, 3, 1, 4)
    dense = [get("w2").T.reshape(M1, P, HD2)]
    for i in range(BLOCKS):
        dense += [get("rw1")[i].T.reshape(M2, P, HD2), get("rw2")[i].T.reshape(M2, P, HD2)]
    partition = np.arange(P)[:, None]
    arrays = {
        "z_t": np.asarray(inputs["r_z"]).T,
        "w1_t": w1.reshape(CHUNKS, P, HD1),
        "dense_t": np.concatenate(dense, axis=0).transpose(1, 0, 2),
        "bn_vectors": np.stack([per_feature(n) for n in ("b", "g", "be", "m", "v")], axis=1),
        "wout_t": columns(get("wout").reshape(-1)),
        "bout": get("bout").reshape(1, 1),
        "categories": (partition // NG + CG * np.arange(CGROUPS)[None, :]).astype(np.float32),
    }
    arrays = {name: np.ascontiguousarray(a) for name, a in arrays.items()}

    nc = bacc.Bacc("TRN2", target_bir_lowering=False, num_devices=1)
    args = [nc.dram_tensor(name, a.shape, mybir.dt.from_np(a.dtype), kind="ExternalInput").ap()
            for name, a in arrays.items()]
    out = nc.dram_tensor("y", (1, B), F32, kind="ExternalOutput").ap()
    mlp_kernel(nc, *args, out)
    r = run_bass_kernel_spmd(nc, [arrays], core_ids=[0])
    return r.results[0]["y"].reshape(-1)
```
